# Optimizing a Trainium2 kernel written in Bass

```python
import numpy as np
import jax
import jax.numpy as jnp

def _softmax(x, axis=-1):
    return jax.nn.softmax(x, axis=axis)

def _gelu(x):
    return jax.nn.gelu(x, approximate=True)

def _silu(x):
    return jax.nn.silu(x)

def _sigmoid(x):
    return jax.nn.sigmoid(x)

def _layernorm(x, axis=-1, eps=1e-05):
    m = jnp.mean(x, axis=axis, keepdims=True)
    v = jnp.var(x, axis=axis, keepdims=True)
    return (x - m) / jnp.sqrt(v + eps)

def _scatter_add(tgt, idx, src, axis=0):
    return tgt.at[idx].add(src)

def _segment_sum(src, seg, n):
    return jax.ops.segment_sum(src, seg, n)
kernel_name = 'mk_adj_preln_d1_adj_r2_73dfbf'

def setup_inputs(seed: int=0):
    np.random.seed(seed)
    _w = jnp.asarray

    def _rec_inputs():
        import jax
        import jax.numpy as jnp
        _gk = jax.random.key(seed)
        x = -0.0005207 + 1.001 * jax.random.normal(jax.random.fold_in(_gk, 1), (8192, 128), jnp.float32)
        _a = jax.random.bernoulli(jax.random.fold_in(_gk, 2), 0.000488281, (8192, 8192))
        _a = jnp.logical_or(_a, jnp.swapaxes(_a, -1, -2))
        _a = jnp.logical_or(_a, jnp.eye(8192, dtype=bool))
        _af = _a.astype(jnp.float32)
        _af = _af * jax.random.uniform(jax.random.fold_in(_gk, 3), (8192, 8192), jnp.float32, 0.05, 6.10351e-05)
        adj = _af
        return (x, adj)
    x, adj = _rec_inputs()

    def _L0_gnn_setup():
        import jax, jax.numpy as jnp
        import numpy as np
        N = 8192
        D = 128
        UNITS = 128
        key = jax.random.key(seed)
        k1, k2, k3 = jax.random.split(key, 3)
        x = jax.random.normal(k1, (N, D), dtype=jnp.float32)
        adj_norm = jax.random.uniform(k2, (N, N), dtype=jnp.float32) / N
        kernel = jax.random.normal(k3, (D, UNITS), dtype=jnp.float32) * (1.0 / np.sqrt(D))
        bias = jnp.zeros((UNITS,), dtype=jnp.float32)
        return {'x': x, 'adj_norm': adj_norm, 'kernel': kernel, 'bias': bias}
    _L0_gnn_all = _L0_gnn_setup()
    _L0_gnn_in = {k: v for k, v in _L0_gnn_all.items() if k in ('kernel', 'bias')}
    del _L0_gnn_all
    return {'x': x, 'adj': adj, 'L0_gnn_kernel': _L0_gnn_in['kernel'], 'L0_gnn_bias': _L0_gnn_in['bias']}

def reference(x, adj, L0_gnn_kernel, L0_gnn_bias):
    import jax
    import jax.numpy as jnp

    def _L0_gnn_ref(x, adj_norm, kernel, bias):
        import jax, jax.numpy as jnp
        import numpy as np
        N = 8192
        D = 128
        UNITS = 128
        agg = adj_norm @ x
        out = agg @ kernel + bias
        return jax.nn.relu(out)
    h = jnp.maximum(_layernorm(x, axis=-1), 0.0)
    x = x + _L0_gnn_ref(h, adj, L0_gnn_kernel, L0_gnn_bias)
    return x

_drawn_inputs = setup_inputs


def setup_inputs(seed=0):
    import zlib

    import numpy as np

    out = dict(_drawn_inputs(seed))
    spreads = {'L0_gnn_bias': (0.0, 0.1)}
    factors = {}
    for name, (base, spread) in spreads.items():
        noise = np.random.default_rng([zlib.crc32(name.encode()), seed]).standard_normal(out[name].shape)
        drawn = base * np.exp(spread * noise) if base else spread * noise
        out[name] = jnp.asarray(drawn.astype(out[name].dtype))
    for name, factor in factors.items():
        out[name] = (out[name] * factor).astype(out[name].dtype)
    return out
```

```python
from contextlib import ExitStack

import concourse.bass as bass
from concourse import mybir

P = 128
F32 = mybir.dt.float32
F32R = mybir.dt.float32r
ALU = mybir.AluOpType
ACT = mybir.ActivationFunctionType

BANK = 512
BANKS = 4
PANEL = BANK * BANKS
PANEL_TILES = PANEL // P
BANK_TILES = BANK // P
EPS = 1e-5

RAW_BUFS = 4
HI_BUFS = 4
LO_BUFS = 2
UNROLL = 4
SUMS_AFTER = 1
OUT_AFTER = 4


def norm_groups(tiles):
    groups, at = [], 0
    for n in [2, 2, 4] + [8] * (tiles // 8):
        n = min(n, tiles - at)
        if n:
            groups.append((at, at + n))
            at += n
    return groups


def gnn_layer(nc, x, adj, weight, bias, out):
    rows, D = x.shape
    U = weight.shape[1]
    TILES = rows // P
    PANELS = rows // PANEL
    CHUNKS = TILES
    GROUPS = norm_groups(TILES)
    assert D == P and U == P and CHUNKS % UNROLL == 0
    assert UNROLL % RAW_BUFS == 0 and UNROLL % HI_BUFS == 0 and UNROLL % LO_BUFS == 0

    STEPS = CHUNKS // UNROLL
    x_rows = x.rearrange("(p t) d -> p t d", p=P)
    out_rows = out.rearrange("(p s b t) u -> p s b t u", p=P, s=PANELS, b=BANKS)
    adj_steps = adj.rearrange("s (g j) p n -> s g j p n", j=UNROLL)

    with ExitStack() as ctx:
        def sb(name, shape, dt=F32):
            return ctx.enter_context(nc.sbuf_tensor(name, shape, dt))

        def sem(name):
            return ctx.enter_context(nc.semaphore(name))

        x_sb = sb("x_sb", [P, TILES, D])
        x_panels = x_sb[:, :, :].rearrange("p (s b t) d -> p s b t d", s=PANELS, b=BANKS)
        h_hi = sb("h_hi", [P, TILES, D], F32R)
        h_lo = sb("h_lo", [P, TILES, D], F32R)
        raw = sb("raw", [P, RAW_BUFS, PANEL])
        hi = sb("hi", [P, HI_BUFS, PANEL], F32R)
        lo = sb("lo", [P, LO_BUFS, PANEL], F32R)
        h_full = sb("h_full", [P, 8, D])
        moments = sb("moments", [P, TILES, 6])
        mean_var = sb("mean_var", [P, TILES, 2])
        deviation = sb("deviation", [P, TILES])
        inverse = sb("inverse", [P, TILES])
        step = sb("step", [P, TILES])
        shift = sb("shift", [P, TILES])
        agg_t = sb("agg_t", [P, BANKS, BANK])
        y = sb("y", [P, BANKS, BANK_TILES, U])
        w_sb = sb("w_sb", [D, U])
        bias_sb = sb("bias_sb", [P, U])
        sums = ctx.enter_context(nc.psum_tensor("sums", [P, BANKS, BANK], F32))
        outs = ctx.enter_context(nc.psum_tensor("outs", [P, BANKS, BANK_TILES, U], F32))

        x_landed = [sem(f"x_landed{g}") for g in range(len(GROUPS))]
        params_landed = sem("params_landed")
        raw_landed = [sem(f"raw_landed{b}") for b in range(RAW_BUFS)]
        stats_done = sem("stats_done")
        var_ready = sem("var_ready")
        root_ready = sem("root_ready")
        scale_ready = sem("scale_ready")
        h_full_ready = sem("h_full_ready")
        h_hi_ready = sem("h_hi_ready")
        h_ready = sem("h_ready")
        hi_ready = sem("hi_ready")
        lo_ready = sem("lo_ready")
        chunk_used = sem("chunk_used")
        sums_ready = sem("sums_ready")
        agg_ready = sem("agg_ready")
        out_ready = sem("out_ready")
        out_free = sem("out_free")
        y_ready = sem("y_ready")
        y_stored = sem("y_stored")

        block = ctx.enter_context(nc.Block())

        @block.sync
        def _(sp):
            def load_chunk(panel, c):
                sp.dma_start(raw[:, c % RAW_BUFS, :], adj[panel, c]).then_inc(raw_landed[c % RAW_BUFS], 16)

            def load_x(g):
                a, b = GROUPS[g]
                sp.dma_start(x_sb[:, a:b, :], x_rows[:, a:b, :]).then_inc(x_landed[g], 16)

            load_x(0)
            for c in range(CHUNKS):
                if c >= RAW_BUFS:
                    sp.wait_ge(lo_ready, c - RAW_BUFS + 1)
                load_chunk(0, c)
                if c == 0:
                    load_x(1)
                    load_x(2)
                    sp.dma_start(w_sb[:, :], weight[:, :]).then_inc(params_landed, 16)
                    sp.dma_start(bias_sb[:, :], bias.rearrange("(a u) -> a u", a=1).broadcast_to([P, U])).then_inc(params_landed, 16)
                elif c < len(GROUPS) - 2:
                    load_x(c + 2)
            with sp.Fori(1, PANELS) as s:
                with sp.Fori(0, STEPS) as g:
                    for j in range(UNROLL):
                        sp.wait_ge(lo_ready, s * CHUNKS + g * UNROLL + (j - RAW_BUFS + 1))
                        sp.dma_start(raw[:, j % RAW_BUFS, :],
                                     adj_steps[bass.ds(s, 1), bass.ds(g, 1), j].rearrange("a b p n -> p (a b n)")
                                     ).then_inc(raw_landed[j % RAW_BUFS], 16)

        @block.gpsimd
        def _(pool):
            def store(panel, b):
                pool.wait_ge(y_ready, panel * BANKS + (b + 1))
                pool.dma_start(out_rows[:, bass.ds(panel, 1), b].rearrange("p s t u -> p (s t) u"),
                               y[:, b]).then_inc(y_stored, 16)

            with pool.Fori(0, PANELS) as s:
                for b in range(BANKS):
                    store(s, b)
            pool.wait_ge(y_stored, 16 * BANKS * PANELS)

        @block.scalar
        def _(act):
            def root(g):
                a, b = GROUPS[g]
                act.wait_ge(var_ready, g + 1)
                nc.scalar.activation(deviation[:, a:b], deviation[:, a:b], ACT.Sqrt).then_inc(root_ready, 1)

            def normalise(g):
                a, b = GROUPS[g]
                act.wait_ge(scale_ready, g + 1)
                if g:
                    act.wait_ge(h_ready, g)
                for t in range(a, b):
                    nc.scalar.activation(h_full[:, t - a, :], x_sb[:, t, :], ACT.Relu, bias=shift[:, t:t + 1],
                                         scale=inverse[:, t:t + 1]).then_inc(h_full_ready, 1)
                act.wait_ge(h_full_ready, b)
                nc.scalar.activation(h_hi[:, a:b, :], h_full[:, 0:b - a, :], ACT.Copy).then_inc(h_hi_ready, 1)

            def take_high(n, j):
                nc.scalar.activation(hi[:, j % HI_BUFS, :], raw[:, j % RAW_BUFS, :], ACT.Copy).then_inc(hi_ready, 1)

            def copy_sums(panel):
                for b in range(BANKS):
                    if b < BANKS - 1:
                        act.wait_ge(sums_ready, panel * (BANKS - 1) + (b + 1))
                    else:
                        act.wait_ge(chunk_used, panel * CHUNKS + CHUNKS)
                    nc.scalar.activation(agg_t[:, b, :], sums[:, b, :], ACT.Copy).then_inc(agg_ready, 1)

            root(0)
            normalise(0)
            at = {}
            for g in range(1, len(GROUPS)):
                first = GROUPS[g][0]
                lead = first - 7 if first > 8 else 0
                at.setdefault(max(lead, 0), []).append((root, g))
                at.setdefault(max(lead + 2, 0) if lead else 1, []).append((normalise, g))
            for c in range(CHUNKS):
                act.wait_ge(raw_landed[c % RAW_BUFS], 16 * (c // RAW_BUFS + 1))
                if c >= HI_BUFS:
                    act.wait_ge(chunk_used, c - HI_BUFS + 1)
                take_high(c, c)
                for what, g in at.get(c, []):
                    what(g)

            with act.Fori(1, PANELS) as s:
                def one(c, j):
                    n = s * CHUNKS + c
                    act.wait_ge(raw_landed[j % RAW_BUFS], (s * CHUNKS + c - j % RAW_BUFS + RAW_BUFS) * (16 // RAW_BUFS))
                    act.wait_ge(chunk_used, n - (HI_BUFS - 1))
                    take_high(n, j)

                for j in range(UNROLL):
                    one(j, j)
                    if j + 1 == SUMS_AFTER:
                        copy_sums(s - 1)
                with act.Fori(1, STEPS) as g:
                    for j in range(UNROLL):
                        one(g * UNROLL + j, j)
            copy_sums(PANELS - 1)

        @block.vector
        def _(dve):
            steps = [0]

            def then(instruction):
                steps[0] += 1
                instruction.then_inc(stats_done, 1)
                dve.wait_ge(stats_done, steps[0])

            def moments_of(g):
                a, b = GROUPS[g]
                dve.wait_ge(x_landed[g], 16)
                for t in range(a, b):
                    last = nc.vector.bn_stats(moments[:, t, :], x_sb[:, t, :])
                then(last)
                for t in range(a, b):
                    last = nc.vector.bn_aggr(mean_var[:, t, :], moments[:, t, :])
                then(last)
                nc.vector.tensor_scalar(deviation[:, a:b], mean_var[:, a:b, 1], EPS, None, ALU.add).then_inc(var_ready, 1)
                then(nc.vector.tensor_scalar(step[:, a:b], mean_var[:, a:b, 1], EPS, None, ALU.add))

            def scales_of(g):
                a, b = GROUPS[g]
                r, v = inverse[:, a:b], step[:, a:b]
                dve.wait_ge(root_ready, g + 1)
                then(nc.vector.reciprocal(r, deviation[:, a:b]))
                then(nc.vector.tensor_tensor(v, v, r, ALU.mult))
                then(nc.vector.tensor_tensor(v, v, r, ALU.mult))
                then(nc.vector.tensor_scalar(v, v, -0.5, 1.5, ALU.mult, ALU.add))
                then(nc.vector.tensor_tensor(r, r, v, ALU.mult))
                nc.vector.scalar_tensor_tensor(shift[:, a:b], mean_var[:, a:b, 0], -1.0, r,
                                               ALU.mult, ALU.mult).then_inc(scale_ready, 1)

            def h_low(g):
                a, b = GROUPS[g]
                dve.wait_ge(h_hi_ready, g + 1)
                nc.vector.tensor_tensor(h_lo[:, a:b, :], h_full[:, 0:b - a, :], h_hi[:, a:b, :].bitcast(F32),
                                        ALU.subtract).then_inc(h_ready, 1)

            def take_low(j):
                nc.vector.tensor_tensor(lo[:, j % LO_BUFS, :], raw[:, j % RAW_BUFS, :],
                                        hi[:, j % HI_BUFS, :].bitcast(F32), ALU.subtract).then_inc(lo_ready, 1)

            def finish(panel, b):
                dve.wait_ge(out_ready, panel * BANKS + (b + 1))
                nc.vector.tensor_tensor(y[:, b], outs[:, b], bias_sb[:, :].rearrange("p (a u) -> p a u", a=1).broadcast_to([P, BANK_TILES, U]),
                                        ALU.add).then_inc(out_free, 1)
                dve.wait_ge(out_free, panel * BANKS + (b + 1 + BANKS))
                nc.vector.scalar_tensor_tensor(
                    y[:, b], y[:, b], 0.0, x_panels[:, bass.ds(panel, 1), b].rearrange("p s t d -> p (s t) d"),
                    ALU.max, ALU.add).then_inc(y_ready, 1)

            dve.sem_inc(out_free, BANKS)
            moments_of(0)
            scales_of(0)
            h_low(0)
            at = {}
            for g in range(1, len(GROUPS)):
                first = GROUPS[g][0]
                lead = first - 7 if first > 8 else 0
                at.setdefault(lead, []).append((moments_of, g))
                at.setdefault(lead + 1, []).append((scales_of, g))
                at.setdefault(lead + 3 if lead else 1, []).append((h_low, g))
            for c in range(CHUNKS):
                for what, g in at.get(c, []):
                    what(g)
                dve.wait_ge(hi_ready, c + 1)
                if c >= LO_BUFS:
                    dve.wait_ge(chunk_used, c - LO_BUFS + 1)
                take_low(c)

            dve.wait_ge(params_landed, 32)
            with dve.Fori(1, PANELS) as s:
                def one(c, j):
                    dve.wait_ge(hi_ready, s * CHUNKS + c + 1)
                    dve.wait_ge(chunk_used, s * CHUNKS + c - (LO_BUFS - 1))
                    take_low(j)

                for j in range(UNROLL):
                    one(j, j)
                    if j + 1 == OUT_AFTER:
                        for b in range(BANKS):
                            finish(s - 1, b)
                with dve.Fori(1, STEPS) as g:
                    for j in range(UNROLL):
                        one(g * UNROLL + j, j)
                dve.wait_ge(y_stored, s * (16 * BANKS))
            for b in range(BANKS):
                finish(PANELS - 1, b)

        @block.tensor
        def _(pe):
            def product(b, c, stationary, moving, j, start=False, stop=False):
                return nc.tensor.matmul(sums[:, b, :], stationary[:, c, :], moving[:, j, b * BANK:(b + 1) * BANK],
                                        start=start, stop=stop)

            pe.wait_ge(params_landed, 32)
            with pe.Fori(0, PANELS) as s:
                for c in range(CHUNKS):
                    if any(a == c for a, _ in GROUPS):
                        pe.wait_ge(h_ready, [a for a, _ in GROUPS].index(c) + 1)
                    h, l = c % HI_BUFS, c % LO_BUFS
                    if c < CHUNKS - 1:
                        pe.wait_ge(hi_ready, s * CHUNKS + (c + 1))
                        for b in range(BANKS):
                            product(b, c, h_lo, hi, h, start=c == 0)
                        for b in range(BANKS):
                            product(b, c, h_hi, hi, h)
                        pe.wait_ge(lo_ready, s * CHUNKS + (c + 1))
                        for b in range(BANKS):
                            last = product(b, c, h_hi, lo, l)
                        last.then_inc(chunk_used, 1)
                    else:
                        pe.wait_ge(lo_ready, s * CHUNKS + (c + 1))
                        for b in range(BANKS):
                            product(b, c, h_lo, hi, h)
                            product(b, c, h_hi, hi, h)
                            last = product(b, c, h_hi, lo, l, stop=True)
                            last.then_inc(sums_ready if b < BANKS - 1 else chunk_used, 1)
                for b in range(BANKS):
                    pe.wait_ge(agg_ready, s * BANKS + (b + 1))
                    pe.wait_ge(out_free, s * BANKS + (b + 1))
                    for t in range(BANK_TILES):
                        last = nc.tensor.matmul(outs[:, b, t, :], agg_t[:, b, t * P:(t + 1) * P], w_sb[:, :],
                                                start=t == 0, stop=t == BANK_TILES - 1)
                    last.then_inc(out_ready, 1)


def kernel(x, adj, L0_gnn_kernel, L0_gnn_bias):
    import numpy as np
    import concourse.bacc as bacc
    from concourse import mybir as mb
    from concourse.bass_utils import run_bass_kernel_spmd

    x, adj = np.asarray(x), np.asarray(adj)
    rows = x.shape[0]
    tiles, panels = rows // P, rows // PANEL
    adj_t = adj.reshape(P, panels, PANEL_TILES, P, tiles).transpose(1, 4, 3, 2, 0)
    arrays = {
        "x_dram": x,
        "adj_dram": np.ascontiguousarray(adj_t).reshape(panels, tiles, P, PANEL),
        "weight_dram": np.asarray(L0_gnn_kernel),
        "bias_dram": np.asarray(L0_gnn_bias),
    }
    arrays = {name: np.ascontiguousarray(a) for name, a in arrays.items()}
    nc = bacc.Bacc("TRN2", target_bir_lowering=False, num_devices=1)
    ins = [nc.dram_tensor(name, a.shape, mb.dt.from_np(a.dtype), kind="ExternalInput").ap() for name, a in arrays.items()]
    out = nc.dram_tensor("out_dram", [rows, arrays["weight_dram"].shape[1]], mb.dt.float32, kind="ExternalOutput").ap()
    gnn_layer(nc, *ins, out)
    r = run_bass_kernel_spmd(nc, [arrays], core_ids=[0])
    return r.results[0]["out_dram"]
```

```python
from contextlib import ExitStack

import concourse.bass as bass
from concourse import mybir

P = 128
F32 = mybir.dt.float32
F32R = mybir.dt.float32r
ALU = mybir.AluOpType
ACT = mybir.ActivationFunctionType

BANK = 512
BANKS = 4
PANEL = BANK * BANKS
BANK_TILES = BANK // P
EPS = 1e-5

UNROLL = 4
RAW_BUFS = UNROLL
HI_BUFS = UNROLL
LO_BUFS = 2
LO_ROW = 32
NATIVE = 8
NORM_TILES = 8
STORE_STEP = 3


def gnn_layer(nc, x, adj, weight, bias, out):
    rows, D = x.shape
    U = weight.shape[1]
    TILES = rows // P
    PANELS = rows // PANEL
    CHUNKS = TILES
    STEPS = CHUNKS // UNROLL
    GROUPS = [(0, 1), (1, 4), (4, NATIVE)] + [(a, a + NORM_TILES) for a in range(NATIVE, TILES, NORM_TILES)]
    FIRST_SPLIT = 3
    SPLITS = len(GROUPS) - FIRST_SPLIT + 1
    FIRST_LATE = len(GROUPS) - 2
    LATE = [(FIRST_LATE, 3), (FIRST_LATE + 1, 8)]
    RESPLIT = 12
    assert D == P and U == P and CHUNKS % UNROLL == 0 and NATIVE % UNROLL == 0 and UNROLL % LO_BUFS == 0
    assert all((step + 5) * UNROLL <= GROUPS[g][0] for g, step in LATE) and LATE[0][1] * UNROLL > NATIVE

    x_rows = x.rearrange("(p t) d -> p t d", p=P)
    out_rows = out.rearrange("(p s b t) u -> p s b t u", p=P, s=PANELS, b=BANKS)
    adj_steps = adj.rearrange("s (g j) p n -> s g j p n", j=UNROLL)

    with ExitStack() as ctx:
        def sb(name, shape, dt=F32):
            return ctx.enter_context(nc.sbuf_tensor(name, shape, dt))

        def sem(name):
            return ctx.enter_context(nc.semaphore(name))

        x_sb = sb("x_sb", [P, TILES, D])
        x_panels = x_sb[:, :, :].rearrange("p (s b t) d -> p s b t d", s=PANELS, b=BANKS)
        h_hi = sb("h_hi", [P, TILES, D], F32R)
        h_lo = sb("h_lo", [P, TILES, D], F32R)
        h_native = sb("h_native", [P, NATIVE, D])
        raw = sb("raw", [P, RAW_BUFS, PANEL])
        hi = sb("hi", [P, HI_BUFS, PANEL], F32R)
        lo = sb("lo", [P, LO_BUFS, PANEL], F32R)
        agg_t = sb("agg_t", [P, BANKS, BANK])
        y = sb("y", [P, BANKS, BANK_TILES, U])
        h_full = y[:, :, :, :].rearrange("p (a b) t u -> p a (b t) u", a=2)
        w_sb = sb("w_sb", [D, U])
        bias_row = sb("bias_row", [1, BANK_TILES, U])
        bias_split = sb("bias_split", [P, BANK_TILES, U], F32R)
        ones = sb("ones", [P, P], F32R)
        moments = sb("moments", [P, NORM_TILES, 6])
        mean_var = sb("mean_var", [P, TILES, 2])
        root = sb("root", [P, TILES])
        variance = sb("variance", [P, TILES])
        newton = sb("newton", [P, TILES])
        scale = sb("scale", [P, TILES])
        shift = sb("shift", [P, TILES])
        sums = ctx.enter_context(nc.psum_tensor("sums", [P, BANKS, BANK], F32))
        outs = ctx.enter_context(nc.psum_tensor("outs", [P, BANKS, BANK_TILES, U], F32))

        x_landed = [sem(f"x_landed{g}") for g in range(len(GROUPS))]
        weight_landed = sem("weight_landed")
        bias_landed = sem("bias_landed")
        raw_landed = [sem(f"raw_landed{j}") for j in range(RAW_BUFS)]
        part_landed = [sem(f"part_landed{b}") for b in range(BANKS - 1)]
        constants_ready = sem("constants_ready")
        bias_ready = sem("bias_ready")
        norm_step = sem("norm_step")
        variance_ready = sem("variance_ready")
        root_ready = sem("root_ready")
        scale_ready = sem("scale_ready")
        h_tile_ready = sem("h_tile_ready")
        h_hi_ready = sem("h_hi_ready")
        h_ready = sem("h_ready")
        hi_ready = sem("hi_ready")
        lo_ready = sem("lo_ready")
        part_hi_ready = sem("part_hi_ready")
        half_hi_ready = sem("half_hi_ready")
        part_lo_ready = sem("part_lo_ready")
        part_sums_ready = sem("part_sums_ready")
        chunk_used = sem("chunk_used")
        agg_ready = sem("agg_ready")
        out_ready = sem("out_ready")
        y_ready = sem("y_ready")
        y_stored = sem("y_stored")

        def columns(b):
            return slice(b * BANK, (b + 1) * BANK)

        def halves(n):
            return slice(n * PANEL // 2, (n + 1) * PANEL // 2)

        def landed(g, panel):
            return panel * (16 * STEPS) + (g * 16 + 16)

        def number(panel, g, j, more):
            return panel * CHUNKS + g * UNROLL + (j + more)

        block = ctx.enter_context(nc.Block())

        @block.sync
        def _(sp):
            def load_x(g):
                a, b = GROUPS[g]
                sp.dma_start(x_sb[:, a:b, :], x_rows[:, a:b, :]).then_inc(x_landed[g], 16)

            def source(panel, g, j):
                if isinstance(panel, int):
                    panel = slice(panel, panel + 1)
                else:
                    panel = bass.ds(panel, 1)
                g = slice(g, g + 1) if isinstance(g, int) else bass.ds(g, 1)
                return adj_steps[panel, g, j].rearrange("a b p n -> p (a b n)")

            def load_chunk(panel, g, j):
                sp.dma_start(raw[:, j, :], source(panel, g, j)).then_inc(raw_landed[j], 16)

            def raw_free(panel, g, j):
                sp.wait_ge(lo_ready, number(panel, g, j, 1 - RAW_BUFS - NATIVE))

            def load_steps(panel, first, last):
                with sp.Fori(first, last) as g:
                    for j in range(UNROLL):
                        raw_free(panel, g, j)
                        load_chunk(panel, g, j)

            def load_last_step(panel):
                for j in range(UNROLL - 1):
                    raw_free(panel, STEPS - 1, j)
                    load_chunk(panel, STEPS - 1, j)
                j = UNROLL - 1
                raw_free(panel, STEPS - 1, j)
                for b in range(BANKS):
                    sp.dma_start(raw[:, j, columns(b)], source(panel, STEPS - 1, j)[:, columns(b)]).then_inc(
                        part_landed[b] if b < BANKS - 1 else raw_landed[j], 16)

            def store(panel):
                for b in range(BANKS):
                    sp.wait_ge(y_ready, panel * BANKS + (b + 1 + BANKS))
                    place = slice(panel, panel + 1) if isinstance(panel, int) else bass.ds(panel, 1)
                    sp.dma_start(out_rows[:, place, b].rearrange("p s t u -> p (s t) u"), y[:, b]).then_inc(y_stored, 16)

            load_x(0)
            load_chunk(0, 0, 0)
            for g in range(1, FIRST_SPLIT):
                load_x(g)
            for c in range(1, NATIVE + UNROLL):
                if c >= RAW_BUFS:
                    sp.wait_ge(chunk_used, c - RAW_BUFS + 1)
                load_chunk(0, c // UNROLL, c % UNROLL)
                if FIRST_SPLIT + c - 1 < len(GROUPS):
                    load_x(FIRST_SPLIT + c - 1)
            load_steps(0, NATIVE // UNROLL + 1, STEPS - 1)
            load_last_step(0)
            with sp.Fori(1, PANELS) as s:
                load_steps(s, 0, STORE_STEP)
                store(s - 1)
                load_steps(s, STORE_STEP, STEPS - 1)
                load_last_step(s)
            store(PANELS - 1)
            sp.wait_ge(y_stored, 16 * BANKS * PANELS)

        @block.gpsimd
        def _(pool):
            nc.gpsimd.memset(ones[:, :].bitcast(F32), 1.0).then_inc(constants_ready, 1)
            nc.gpsimd.memset(bias_split[:, :, :].bitcast(F32), 0.0).then_inc(constants_ready, 1)

        @block.scalar
        def _(act):
            act.dma_start(w_sb[:, :], weight[:, :]).then_inc(weight_landed, 16)
            act.dma_start(bias_row[:, :, :], bias.rearrange("(a t u) -> a t u", a=1, t=1).broadcast_to([1, BANK_TILES, U])
                          ).then_inc(bias_landed, 16)
            act.preload_act_table(ACT.Sqrt)

            def take_root(g):
                a, b = GROUPS[g]
                act.wait_ge(variance_ready, g + 1)
                nc.scalar.activation(root[:, a:b], variance[:, a:b], ACT.Sqrt).then_inc(root_ready, 1)

            def normalise(g, to):
                a, b = GROUPS[g]
                act.wait_ge(scale_ready, g + 1)
                for t in range(a, b):
                    nc.scalar.activation(to[:, t - a, :], x_sb[:, t, :], ACT.Relu, bias=shift[:, t:t + 1],
                                         scale=scale[:, t:t + 1]).then_inc(h_tile_ready, 1)

            def normalise_and_split(g):
                if g > FIRST_SPLIT + 1:
                    act.wait_ge(h_ready, g - FIRST_SPLIT - 1)
                normalise(g, h_full[:, g % 2])
                a, b = GROUPS[g]
                act.wait_ge(h_tile_ready, b)
                nc.scalar.activation(h_hi[:, a:b, :], h_full[:, g % 2], ACT.Copy).then_inc(h_hi_ready, 1)

            def take_high(panel, g, j):
                act.wait_ge(raw_landed[j], landed(g, panel))
                act.wait_ge(chunk_used, number(panel, g, j, 1 - HI_BUFS))
                nc.scalar.activation(hi[:, j, :], raw[:, j, :], ACT.Copy).then_inc(hi_ready, 1)

            def steps(panel, first, last):
                with act.Fori(first, last) as g:
                    for j in range(UNROLL):
                        take_high(panel, g, j)

            def last_step(panel):
                for j in range(UNROLL - 2):
                    take_high(panel, STEPS - 1, j)
                j = UNROLL - 2
                act.wait_ge(raw_landed[j], landed(STEPS - 1, panel))
                act.wait_ge(chunk_used, number(panel, STEPS - 1, j, 1 - HI_BUFS))
                for half, signal in enumerate([half_hi_ready, hi_ready]):
                    nc.scalar.activation(hi[:, j, halves(half)], raw[:, j, halves(half)], ACT.Copy).then_inc(signal, 1)
                j = UNROLL - 1
                act.wait_ge(chunk_used, number(panel, STEPS - 1, j, 1 - HI_BUFS))
                for b in range(BANKS):
                    last = b == BANKS - 1
                    if last:
                        act.wait_ge(raw_landed[j], landed(STEPS - 1, panel))
                    else:
                        act.wait_ge(part_landed[b], panel * 16 + 16)
                    nc.scalar.activation(hi[:, j, columns(b)], raw[:, j, columns(b)], ACT.Copy).then_inc(
                        hi_ready if last else part_hi_ready, 1)

            def copy_sums(panel):
                for b in range(BANKS):
                    if b < BANKS - 1:
                        act.wait_ge(part_sums_ready, panel * (BANKS - 1) + (b + 1))
                    else:
                        act.wait_ge(chunk_used, panel * CHUNKS + CHUNKS)
                    nc.scalar.activation(agg_t[:, b, :], sums[:, b, :], ACT.Copy).then_inc(agg_ready, 1)

            for g in range(FIRST_SPLIT):
                take_root(g)
                normalise(g, h_native[:, GROUPS[g][0]:, :])
            take_root(FIRST_SPLIT)
            for g in range(FIRST_SPLIT, FIRST_LATE):
                if g + 1 < FIRST_LATE:
                    take_root(g + 1)
                normalise_and_split(g)
            at = NATIVE // UNROLL
            for g, step in LATE:
                steps(0, at, step + 1)
                take_root(g)
                steps(0, step + 1, step + 3)
                normalise_and_split(g)
                at = step + 3
            steps(0, at, RESPLIT)
            nc.scalar.activation(h_hi[:, 0:NATIVE, :], h_native[:, :, :], ACT.Copy).then_inc(h_hi_ready, 1)
            steps(0, RESPLIT, STEPS - 1)
            last_step(0)
            with act.Fori(1, PANELS) as s:
                take_high(s, 0, 0)
                copy_sums(s - 1)
                for j in range(1, UNROLL):
                    take_high(s, 0, j)
                steps(s, 1, STEPS - 1)
                last_step(s)
            copy_sums(PANELS - 1)

        @block.vector
        def _(dve):
            done = [0]

            def then(instruction):
                done[0] += 1
                instruction.then_inc(norm_step, 1)
                dve.wait_ge(norm_step, done[0])

            def variances(g):
                a, b = GROUPS[g]
                dve.wait_ge(x_landed[g], 16)
                for t in range(a, b):
                    last = nc.vector.bn_stats(moments[:, t - a, :], x_sb[:, t, :])
                then(last)
                for t in range(a, b):
                    last = nc.vector.bn_aggr(mean_var[:, t, :], moments[:, t - a, :])
                then(last)
                nc.vector.tensor_scalar(variance[:, a:b], mean_var[:, a:b, 1], EPS, None, ALU.add).then_inc(variance_ready, 1)

            def scales(g):
                a, b = GROUPS[g]
                r, n = scale[:, a:b], newton[:, a:b]
                dve.wait_ge(root_ready, g + 1)
                then(nc.vector.reciprocal(r, root[:, a:b]))
                then(nc.vector.tensor_tensor(n, variance[:, a:b], r, ALU.mult))
                then(nc.vector.tensor_tensor(n, n, r, ALU.mult))
                then(nc.vector.tensor_scalar(n, n, -0.5, 1.5, ALU.mult, ALU.add))
                then(nc.vector.tensor_tensor(r, r, n, ALU.mult))
                nc.vector.scalar_tensor_tensor(shift[:, a:b], mean_var[:, a:b, 0], -1.0, r,
                                               ALU.mult, ALU.mult).then_inc(scale_ready, 1)

            def h_low(tiles, full, n):
                dve.wait_ge(h_hi_ready, n)
                nc.vector.tensor_tensor(h_lo[:, tiles, :], full, h_hi[:, tiles, :].bitcast(F32),
                                        ALU.subtract).then_inc(h_ready, 1)

            def group_low(g):
                h_low(slice(*GROUPS[g]), h_full[:, g % 2], g - FIRST_SPLIT + 1)

            def take_low(panel, g, j):
                dve.wait_ge(hi_ready, number(panel, g, j, 1 - NATIVE))
                dve.wait_ge(chunk_used, number(panel, g, j, 1 - LO_BUFS))
                nc.vector.tensor_tensor(lo[:, j % LO_BUFS, :], raw[:, j, :], hi[:, j, :].bitcast(F32),
                                        ALU.subtract).then_inc(lo_ready, 1)

            def steps(panel, first, last):
                with dve.Fori(first, last) as g:
                    for j in range(UNROLL):
                        take_low(panel, g, j)

            def last_step(panel):
                for j in range(UNROLL - 2):
                    take_low(panel, STEPS - 1, j)
                j = UNROLL - 2
                dve.wait_ge(chunk_used, number(panel, STEPS - 1, j, 1 - LO_BUFS))
                dve.wait_ge(half_hi_ready, panel + 1)
                nc.vector.tensor_tensor(lo[:, j % LO_BUFS, halves(0)], raw[:, j, halves(0)],
                                        hi[:, j, halves(0)].bitcast(F32), ALU.subtract)
                dve.wait_ge(hi_ready, number(panel, STEPS - 1, j, 1 - NATIVE))
                nc.vector.tensor_tensor(lo[:, j % LO_BUFS, halves(1)], raw[:, j, halves(1)],
                                        hi[:, j, halves(1)].bitcast(F32), ALU.subtract).then_inc(lo_ready, 1)
                j = UNROLL - 1
                dve.wait_ge(chunk_used, number(panel, STEPS - 1, j, 1 - LO_BUFS))
                for b in range(BANKS):
                    last = b == BANKS - 1
                    if last:
                        dve.wait_ge(hi_ready, number(panel, STEPS - 1, j, 1 - NATIVE))
                    else:
                        dve.wait_ge(part_hi_ready, panel * (BANKS - 1) + (b + 1))
                    nc.vector.tensor_tensor(lo[:, j % LO_BUFS, columns(b)], raw[:, j, columns(b)],
                                            hi[:, j, columns(b)].bitcast(F32), ALU.subtract).then_inc(
                        lo_ready if last else part_lo_ready, 1)

            def finish(panel, b):
                place = slice(panel, panel + 1) if isinstance(panel, int) else bass.ds(panel, 1)
                dve.wait_ge(out_ready, panel * BANKS + (b + 1))
                nc.vector.scalar_tensor_tensor(
                    y[:, b], outs[:, b], 0.0, x_panels[:, place, b].rearrange("p s t d -> p (s t) d"),
                    ALU.max, ALU.add).then_inc(y_ready, 1)

            dve.sem_inc(y_ready, BANKS)
            for g in range(FIRST_SPLIT):
                variances(g)
                scales(g)
            variances(FIRST_SPLIT)
            scales(FIRST_SPLIT)
            variances(FIRST_SPLIT + 1)
            for g in range(FIRST_SPLIT, FIRST_LATE):
                if g + 1 < FIRST_LATE:
                    scales(g + 1)
                if g + 2 < FIRST_LATE:
                    variances(g + 2)
                group_low(g)
            dve.wait_ge(bias_landed, 16)
            dve.wait_ge(constants_ready, 2)
            nc.vector.tensor_copy(bias_split[0:1], bias_row[:, :, :]).then_inc(bias_ready, 1)
            dve.wait_ge(bias_ready, 1)
            nc.vector.tensor_tensor(bias_split[LO_ROW:LO_ROW + 1], bias_row[:, :, :], bias_split[0:1].bitcast(F32),
                                    ALU.subtract).then_inc(bias_ready, 1)
            at = NATIVE // UNROLL
            for g, step in LATE:
                steps(0, at, step)
                variances(g)
                steps(0, step, step + 2)
                scales(g)
                steps(0, step + 2, step + 4)
                group_low(g)
                at = step + 4
            steps(0, at, RESPLIT + 1)
            h_low(slice(0, NATIVE), h_native[:, :, :], SPLITS)
            steps(0, RESPLIT + 1, STEPS - 1)
            last_step(0)
            with dve.Fori(1, PANELS) as s:
                steps(s, 0, 1)
                for j in range(UNROLL):
                    take_low(s, 1, j)
                    finish(s - 1, j)
                steps(s, 2, STEPS - 1)
                last_step(s)
                dve.wait_ge(y_stored, s * (16 * BANKS))
            for b in range(BANKS):
                finish(PANELS - 1, b)

        @block.tensor
        def _(pe):
            def products(b, c, stationary, moving, j):
                return nc.tensor.matmul(sums[:, b, :], stationary[:, c, :], moving[:, j, columns(b)],
                                        start=c == 0 and stationary is not h_hi, stop=c == CHUNKS - 1 and moving is lo)

            def native_chunk(c):
                pe.wait_ge(h_tile_ready, c + 1)
                pe.wait_ge(raw_landed[c % RAW_BUFS], landed(c // UNROLL, 0))
                for b in range(BANKS):
                    last = products(b, c, h_native, raw, c % RAW_BUFS)
                last.then_inc(chunk_used, 1)

            def chunk(panel, c):
                pe.wait_ge(hi_ready, number(panel, 0, c, 1 - NATIVE))
                for b in range(BANKS):
                    products(b, c, h_lo, hi, c % HI_BUFS)
                for b in range(BANKS):
                    products(b, c, h_hi, hi, c % HI_BUFS)
                pe.wait_ge(lo_ready, number(panel, 0, c, 1 - NATIVE))
                for b in range(BANKS):
                    last = products(b, c, h_hi, lo, c % LO_BUFS)
                last.then_inc(chunk_used, 1)

            def last_chunk(panel):
                c = CHUNKS - 1
                for b in range(BANKS):
                    last = b == BANKS - 1
                    part = panel * (BANKS - 1) + (b + 1)
                    pe.wait_ge(hi_ready if last else part_hi_ready, number(panel, 0, c, 1 - NATIVE) if last else part)
                    products(b, c, h_lo, hi, c % HI_BUFS)
                    products(b, c, h_hi, hi, c % HI_BUFS)
                    pe.wait_ge(lo_ready if last else part_lo_ready, number(panel, 0, c, 1 - NATIVE) if last else part)
                    products(b, c, h_hi, lo, c % LO_BUFS).then_inc(chunk_used if last else part_sums_ready, 1)

            def outputs(panel):
                for b in range(BANKS):
                    pe.wait_ge(y_ready, panel * BANKS + (b + 1))
                    nc.tensor.matmul(outs[:, b], ones[:, :], bias_split[:, :, :], start=True, stop=False)
                for b in range(BANKS):
                    pe.wait_ge(agg_ready, panel * BANKS + (b + 1))
                    for t in range(BANK_TILES):
                        last = nc.tensor.matmul(outs[:, b, t, :], agg_t[:, b, t * P:(t + 1) * P], w_sb[:, :],
                                                start=False, stop=t == BANK_TILES - 1)
                    last.then_inc(out_ready, 1)

            for c in range(NATIVE):
                native_chunk(c)
            for c in range(NATIVE, CHUNKS - 1):
                if c % NORM_TILES == 0:
                    pe.wait_ge(h_ready, (c - NATIVE) // NORM_TILES + 1)
                chunk(0, c)
            last_chunk(0)
            pe.wait_ge(weight_landed, 16)
            pe.wait_ge(bias_ready, 2)
            outputs(0)
            pe.wait_ge(h_ready, SPLITS)
            with pe.Fori(1, PANELS) as s:
                for c in range(CHUNKS - 1):
                    chunk(s, c)
                last_chunk(s)
                outputs(s)


def kernel(x, adj, L0_gnn_kernel, L0_gnn_bias):
    import numpy as np
    import concourse.bacc as bacc
    from concourse import mybir as mb
    from concourse.bass_utils import run_bass_kernel_spmd

    x, adj = np.asarray(x), np.asarray(adj)
    rows = x.shape[0]
    tiles, panels = rows // P, rows // PANEL
    adj_t = adj.reshape(P, panels, PANEL // P, P, tiles).transpose(1, 4, 3, 2, 0)
    arrays = {
        "x_dram": x,
        "adj_dram": np.ascontiguousarray(adj_t).reshape(panels, tiles, P, PANEL),
        "weight_dram": np.asarray(L0_gnn_kernel),
        "bias_dram": np.asarray(L0_gnn_bias),
    }
    arrays = {name: np.ascontiguousarray(a) for name, a in arrays.items()}
    nc = bacc.Bacc("TRN2", target_bir_lowering=False, num_devices=1)
    ins = [nc.dram_tensor(name, a.shape, mb.dt.from_np(a.dtype), kind="ExternalInput").ap() for name, a in arrays.items()]
    out = nc.dram_tensor("out_dram", [rows, arrays["weight_dram"].shape[1]], mb.dt.float32, kind="ExternalOutput").ap()
    gnn_layer(nc, *ins, out)
    r = run_bass_kernel_spmd(nc, [arrays], core_ids=[0])
    return r.results[0]["out_dram"]
```

```python
from contextlib import ExitStack

import concourse.bass as bass
from concourse import mybir

P = 128
F32 = mybir.dt.float32
F32R = mybir.dt.float32r
ALU = mybir.AluOpType
ACT = mybir.ActivationFunctionType

BANK = 512
BANKS = 4
PANEL = BANK * BANKS
BANK_TILES = BANK // P
EPS = 1e-5

UNROLL = 4
RAW_BUFS = UNROLL
HI_BUFS = UNROLL
LO_BUFS = 2
LO_ROW = 32
NATIVE = 8
NORM_TILES = 8
EARLY_GROUPS = 3
STORE_STEP = 3


def gnn_layer(nc, x, adj, weight, bias, out):
    rows, D = x.shape
    U = weight.shape[1]
    TILES = rows // P
    PANELS = rows // PANEL
    CHUNKS = TILES
    STEPS = CHUNKS // UNROLL
    GROUPS = [(0, 1), (1, 4), (4, NATIVE)] + [(a, a + NORM_TILES) for a in range(NATIVE, TILES, NORM_TILES)]
    FIRST_SPLIT = 3
    SPLITS = len(GROUPS) - FIRST_SPLIT + 1
    FOLLOWING, at = {}, NATIVE // UNROLL
    for g in range(FIRST_SPLIT, len(GROUPS)):
        n = 1 if g >= FIRST_SPLIT + EARLY_GROUPS else 0
        FOLLOWING[g] = (at, at + n, at + 2 * n)
        at += 2 * n
    RESPLIT = at + 2
    assert D == P and U == P and CHUNKS % UNROLL == 0 and NATIVE % UNROLL == 0 and UNROLL % LO_BUFS == 0
    assert all(GROUPS[g][0] >= FOLLOWING[g][0] * UNROLL for g in FOLLOWING) and RESPLIT < STEPS - 1

    x_rows = x.rearrange("(p t) d -> p t d", p=P)
    out_rows = out.rearrange("(p s b t) u -> p s b t u", p=P, s=PANELS, b=BANKS)
    adj_steps = adj.rearrange("s (g j) p n -> s g j p n", j=UNROLL)

    with ExitStack() as ctx:
        def sb(name, shape, dt=F32):
            return ctx.enter_context(nc.sbuf_tensor(name, shape, dt))

        def sem(name):
            return ctx.enter_context(nc.semaphore(name))

        x_sb = sb("x_sb", [P, TILES, D])
        x_panels = x_sb[:, :, :].rearrange("p (s b t) d -> p s b t d", s=PANELS, b=BANKS)
        h_hi = sb("h_hi", [P, TILES, D], F32R)
        h_lo = sb("h_lo", [P, TILES, D], F32R)
        h_native = sb("h_native", [P, NATIVE, D])
        raw = sb("raw", [P, RAW_BUFS, PANEL])
        hi = sb("hi", [P, HI_BUFS, PANEL], F32R)
        lo = sb("lo", [P, LO_BUFS, PANEL], F32R)
        agg_t = sb("agg_t", [P, BANKS, BANK])
        y = sb("y", [P, BANKS, BANK_TILES, U])
        h_full = y[:, :, :, :].rearrange("p (a b) t u -> p a (b t) u", a=2)
        w_sb = sb("w_sb", [D, U])
        bias_row = sb("bias_row", [1, BANK_TILES, U])
        bias_split = sb("bias_split", [P, BANK_TILES, U], F32R)
        ones = sb("ones", [P, P], F32R)
        moments = sb("moments", [P, NORM_TILES, 6])
        mean_var = sb("mean_var", [P, TILES, 2])
        root = sb("root", [P, TILES])
        variance = sb("variance", [P, TILES])
        newton = sb("newton", [P, TILES])
        scale = sb("scale", [P, TILES])
        shift = sb("shift", [P, TILES])
        sums = ctx.enter_context(nc.psum_tensor("sums", [P, BANKS, BANK], F32))
        outs = ctx.enter_context(nc.psum_tensor("outs", [P, BANKS, BANK_TILES, U], F32))

        x_landed = [sem(f"x_landed{g}") for g in range(len(GROUPS))]
        weight_landed = sem("weight_landed")
        bias_landed = sem("bias_landed")
        raw_landed = [sem(f"raw_landed{j}") for j in range(RAW_BUFS)]
        part_landed = [sem(f"part_landed{b}") for b in range(BANKS - 1)]
        constants_ready = sem("constants_ready")
        bias_ready = sem("bias_ready")
        norm_step = sem("norm_step")
        variance_ready = sem("variance_ready")
        root_ready = sem("root_ready")
        scale_ready = sem("scale_ready")
        h_tile_ready = sem("h_tile_ready")
        h_hi_ready = sem("h_hi_ready")
        h_ready = sem("h_ready")
        hi_ready = sem("hi_ready")
        lo_ready = sem("lo_ready")
        part_hi_ready = sem("part_hi_ready")
        part_lo_ready = sem("part_lo_ready")
        part_sums_ready = sem("part_sums_ready")
        chunk_used = sem("chunk_used")
        agg_ready = sem("agg_ready")
        out_ready = sem("out_ready")
        y_ready = sem("y_ready")
        y_stored = sem("y_stored")

        def one(i):
            return slice(i, i + 1) if isinstance(i, int) else bass.ds(i, 1)

        def columns(b):
            return slice(b * BANK, (b + 1) * BANK)

        def half_banks(half):
            return range(half * BANKS // 2, (half + 1) * BANKS // 2)

        def halves(n):
            return slice(n * PANEL // 2, (n + 1) * PANEL // 2)

        def landed(g, panel):
            return panel * (16 * STEPS) + (g * 16 + 16)

        def number(panel, g, j, more):
            return panel * CHUNKS + g * UNROLL + (j + more)

        def half_done(panel, g, j, half):
            return panel * (2 * CHUNKS) + g * (2 * UNROLL) + (2 * (j - NATIVE) + half + 1)

        block = ctx.enter_context(nc.Block())

        @block.sync
        def _(sp):
            def load_x(g):
                a, b = GROUPS[g]
                sp.dma_start(x_sb[:, a:b, :], x_rows[:, a:b, :]).then_inc(x_landed[g], 16)

            def source(panel, g, j):
                return adj_steps[one(panel), one(g), j].rearrange("a b p n -> p (a b n)")

            def load_chunk(panel, g, j):
                sp.dma_start(raw[:, j, :], source(panel, g, j)).then_inc(raw_landed[j], 16)

            def raw_free(panel, g, j):
                sp.wait_ge(lo_ready, half_done(panel, g, j - RAW_BUFS, 1))

            def load_steps(panel, first, last):
                with sp.Fori(first, last) as g:
                    for j in range(UNROLL):
                        raw_free(panel, g, j)
                        load_chunk(panel, g, j)

            def load_last_step(panel):
                for j in range(UNROLL - 1):
                    raw_free(panel, STEPS - 1, j)
                    load_chunk(panel, STEPS - 1, j)
                j = UNROLL - 1
                raw_free(panel, STEPS - 1, j)
                for b in range(BANKS):
                    sp.dma_start(raw[:, j, columns(b)], source(panel, STEPS - 1, j)[:, columns(b)]).then_inc(
                        part_landed[b] if b < BANKS - 1 else raw_landed[j], 16)

            def store(panel):
                for b in range(BANKS):
                    sp.wait_ge(y_ready, panel * BANKS + (b + 1 + BANKS))
                    sp.dma_start(out_rows[:, one(panel), b].rearrange("p s t u -> p (s t) u"), y[:, b]).then_inc(y_stored, 16)

            load_x(0)
            load_chunk(0, 0, 0)
            for g in range(1, FIRST_SPLIT):
                load_x(g)
            for c in range(1, NATIVE + UNROLL):
                if c >= RAW_BUFS:
                    sp.wait_ge(chunk_used, c - RAW_BUFS + 1)
                load_chunk(0, c // UNROLL, c % UNROLL)
                if FIRST_SPLIT + c - 1 < len(GROUPS):
                    load_x(FIRST_SPLIT + c - 1)
            load_steps(0, NATIVE // UNROLL + 1, STEPS - 1)
            load_last_step(0)
            with sp.Fori(1, PANELS) as s:
                load_steps(s, 0, STORE_STEP)
                store(s - 1)
                load_steps(s, STORE_STEP, STEPS - 1)
                load_last_step(s)
            store(PANELS - 1)
            sp.wait_ge(y_stored, 16 * BANKS * PANELS)

        @block.gpsimd
        def _(pool):
            nc.gpsimd.memset(ones[:, :].bitcast(F32), 1.0).then_inc(constants_ready, 1)
            nc.gpsimd.memset(bias_split[:, :, :].bitcast(F32), 0.0).then_inc(constants_ready, 1)

        @block.scalar
        def _(act):
            act.preload_act_table(ACT.Sqrt)
            act.dma_start(w_sb[:, :], weight[:, :]).then_inc(weight_landed, 16)
            act.dma_start(bias_row[:, :, :], bias.rearrange("(a t u) -> a t u", a=1, t=1).broadcast_to([1, BANK_TILES, U])
                          ).then_inc(bias_landed, 16)

            def take_root(g):
                a, b = GROUPS[g]
                act.wait_ge(variance_ready, g + 1)
                nc.scalar.activation(root[:, a:b], variance[:, a:b], ACT.Sqrt).then_inc(root_ready, 1)

            def normalise(g, to, first, last):
                a, _ = GROUPS[g]
                act.wait_ge(scale_ready, g + 1)
                for t in range(a + first, a + last):
                    nc.scalar.activation(to[:, t - a, :], x_sb[:, t, :], ACT.Relu, bias=shift[:, t:t + 1],
                                         scale=scale[:, t:t + 1]).then_inc(h_tile_ready, 1)

            def group_high(g):
                a, b = GROUPS[g]
                act.wait_ge(h_tile_ready, b)
                nc.scalar.activation(h_hi[:, a:b, :], h_full[:, g % 2], ACT.Copy).then_inc(h_hi_ready, 1)

            def take_high(panel, g, j):
                act.wait_ge(raw_landed[j], landed(g, panel))
                act.wait_ge(chunk_used, number(panel, g, j, 1 - HI_BUFS))
                for half in range(2):
                    nc.scalar.activation(hi[:, j, halves(half)], raw[:, j, halves(half)], ACT.Copy).then_inc(hi_ready, 1)

            def steps(panel, first, last):
                if first < last:
                    with act.Fori(first, last) as g:
                        for j in range(UNROLL):
                            take_high(panel, g, j)

            def last_step(panel):
                for j in range(UNROLL - 1):
                    take_high(panel, STEPS - 1, j)
                j = UNROLL - 1
                act.wait_ge(chunk_used, number(panel, STEPS - 1, j, 1 - HI_BUFS))
                for b in range(BANKS):
                    last = b == BANKS - 1
                    if last:
                        act.wait_ge(raw_landed[j], landed(STEPS - 1, panel))
                    else:
                        act.wait_ge(part_landed[b], panel * 16 + 16)
                    nc.scalar.activation(hi[:, j, columns(b)], raw[:, j, columns(b)], ACT.Copy).then_inc(
                        hi_ready if b % 2 else part_hi_ready, 1)

            def copy_sums(panel):
                for b in range(BANKS):
                    if b < BANKS - 1:
                        act.wait_ge(part_sums_ready, panel * (BANKS - 1) + (b + 1))
                    else:
                        act.wait_ge(chunk_used, panel * CHUNKS + CHUNKS)
                    nc.scalar.activation(agg_t[:, b, :], sums[:, b, :], ACT.Copy).then_inc(agg_ready, 1)

            for g in range(FIRST_SPLIT):
                take_root(g)
                a, b = GROUPS[g]
                normalise(g, h_native[:, a:b, :], 0, b - a)
            take_root(FIRST_SPLIT)
            for g in range(FIRST_SPLIT, len(GROUPS)):
                if g + 1 < len(GROUPS):
                    take_root(g + 1)
                if g > FIRST_SPLIT + 1:
                    act.wait_ge(h_ready, g - FIRST_SPLIT - 1)
                start, middle, end = FOLLOWING[g]
                normalise(g, h_full[:, g % 2], 0, NORM_TILES // 2)
                steps(0, start, middle)
                normalise(g, h_full[:, g % 2], NORM_TILES // 2, NORM_TILES)
                group_high(g)
                steps(0, middle, end)
            steps(0, RESPLIT - 2, RESPLIT)
            nc.scalar.activation(h_hi[:, 0:NATIVE, :], h_native[:, :, :], ACT.Copy).then_inc(h_hi_ready, 1)
            steps(0, RESPLIT, STEPS - 1)
            last_step(0)
            with act.Fori(1, PANELS) as s:
                take_high(s, 0, 0)
                copy_sums(s - 1)
                for j in range(1, UNROLL):
                    take_high(s, 0, j)
                steps(s, 1, STEPS - 1)
                last_step(s)
            copy_sums(PANELS - 1)

        @block.vector
        def _(dve):
            done = [0]

            def then(instruction):
                done[0] += 1
                instruction.then_inc(norm_step, 1)
                dve.wait_ge(norm_step, done[0])

            def variances(g):
                a, b = GROUPS[g]
                dve.wait_ge(x_landed[g], 16)
                for t in range(a, b):
                    last = nc.vector.bn_stats(moments[:, t - a, :], x_sb[:, t, :])
                then(last)
                for t in range(a, b):
                    last = nc.vector.bn_aggr(mean_var[:, t, :], moments[:, t - a, :])
                then(last)
                nc.vector.tensor_scalar(variance[:, a:b], mean_var[:, a:b, 1], EPS, None, ALU.add).then_inc(variance_ready, 1)

            def scales(g):
                a, b = GROUPS[g]
                r, n = scale[:, a:b], newton[:, a:b]
                dve.wait_ge(root_ready, g + 1)
                then(nc.vector.reciprocal(r, root[:, a:b]))
                then(nc.vector.tensor_tensor(n, variance[:, a:b], r, ALU.mult))
                then(nc.vector.tensor_tensor(n, n, r, ALU.mult))
                then(nc.vector.tensor_scalar(n, n, -0.5, 1.5, ALU.mult, ALU.add))
                then(nc.vector.tensor_tensor(r, r, n, ALU.mult))
                nc.vector.scalar_tensor_tensor(shift[:, a:b], mean_var[:, a:b, 0], -1.0, r,
                                               ALU.mult, ALU.mult).then_inc(scale_ready, 1)

            def h_low(tiles, full, n):
                dve.wait_ge(h_hi_ready, n)
                nc.vector.tensor_tensor(h_lo[:, tiles, :], full, h_hi[:, tiles, :].bitcast(F32),
                                        ALU.subtract).then_inc(h_ready, 1)

            def group_low(g):
                h_low(slice(*GROUPS[g]), h_full[:, g % 2], g - FIRST_SPLIT + 1)

            def take_low(panel, g, j):
                dve.wait_ge(chunk_used, number(panel, g, j, 1 - LO_BUFS))
                for half in range(2):
                    dve.wait_ge(hi_ready, half_done(panel, g, j, half))
                    nc.vector.tensor_tensor(lo[:, j % LO_BUFS, halves(half)], raw[:, j, halves(half)],
                                            hi[:, j, halves(half)].bitcast(F32), ALU.subtract).then_inc(lo_ready, 1)

            def steps(panel, first, last):
                if first < last:
                    with dve.Fori(first, last) as g:
                        for j in range(UNROLL):
                            take_low(panel, g, j)

            def last_step(panel):
                for j in range(UNROLL - 1):
                    take_low(panel, STEPS - 1, j)
                j = UNROLL - 1
                dve.wait_ge(chunk_used, number(panel, STEPS - 1, j, 1 - LO_BUFS))
                for b in range(BANKS):
                    if b % 2:
                        dve.wait_ge(hi_ready, half_done(panel, STEPS - 1, j, b // 2))
                    else:
                        dve.wait_ge(part_hi_ready, panel * (BANKS // 2) + (b // 2 + 1))
                    nc.vector.tensor_tensor(lo[:, j % LO_BUFS, columns(b)], raw[:, j, columns(b)],
                                            hi[:, j, columns(b)].bitcast(F32), ALU.subtract).then_inc(
                        lo_ready if b % 2 else part_lo_ready, 1)

            def finish(panel, b):
                dve.wait_ge(out_ready, panel * BANKS + (b + 1))
                nc.vector.scalar_tensor_tensor(
                    y[:, b], outs[:, b], 0.0, x_panels[:, one(panel), b].rearrange("p s t d -> p (s t) d"),
                    ALU.max, ALU.add).then_inc(y_ready, 1)

            dve.sem_inc(y_ready, BANKS)
            for g in range(FIRST_SPLIT):
                variances(g)
                scales(g)
            variances(FIRST_SPLIT)
            scales(FIRST_SPLIT)
            variances(FIRST_SPLIT + 1)
            for g in range(FIRST_SPLIT, len(GROUPS)):
                if g + 1 < len(GROUPS):
                    scales(g + 1)
                start, middle, end = FOLLOWING[g]
                steps(0, start, middle)
                if g + 2 < len(GROUPS):
                    variances(g + 2)
                group_low(g)
                steps(0, middle, end)
            dve.wait_ge(bias_landed, 16)
            dve.wait_ge(constants_ready, 2)
            nc.vector.tensor_copy(bias_split[0:1], bias_row[:, :, :]).then_inc(bias_ready, 1)
            dve.wait_ge(bias_ready, 1)
            nc.vector.tensor_tensor(bias_split[LO_ROW:LO_ROW + 1], bias_row[:, :, :], bias_split[0:1].bitcast(F32),
                                    ALU.subtract).then_inc(bias_ready, 1)
            steps(0, RESPLIT - 2, RESPLIT + 1)
            h_low(slice(0, NATIVE), h_native[:, :, :], SPLITS)
            steps(0, RESPLIT + 1, STEPS - 1)
            last_step(0)
            with dve.Fori(1, PANELS) as s:
                steps(s, 0, 1)
                for j in range(UNROLL):
                    take_low(s, 1, j)
                    finish(s - 1, j)
                steps(s, 2, STEPS - 1)
                last_step(s)
                dve.wait_ge(y_stored, s * (16 * BANKS))
            for b in range(BANKS):
                finish(PANELS - 1, b)

        @block.tensor
        def _(pe):
            BIAS_CHUNK = CHUNKS - 4 * UNROLL

            def products(b, c, stationary, moving, j):
                return nc.tensor.matmul(sums[:, b, :], stationary[:, c, :], moving[:, j, columns(b)],
                                        start=c == 0 and stationary is not h_hi, stop=c == CHUNKS - 1 and moving is lo)

            def native_chunk(c):
                pe.wait_ge(h_tile_ready, c + 1)
                pe.wait_ge(raw_landed[c % RAW_BUFS], landed(c // UNROLL, 0))
                for b in range(BANKS):
                    last = products(b, c, h_native, raw, c % RAW_BUFS)
                last.then_inc(chunk_used, 1)

            def chunk(panel, c):
                for half in range(2):
                    pe.wait_ge(hi_ready, half_done(panel, 0, c, half))
                    for stationary in (h_lo, h_hi):
                        for b in half_banks(half):
                            products(b, c, stationary, hi, c % HI_BUFS)
                for half in range(2):
                    pe.wait_ge(lo_ready, half_done(panel, 0, c, half))
                    for b in half_banks(half):
                        last = products(b, c, h_hi, lo, c % LO_BUFS)
                last.then_inc(chunk_used, 1)

            def last_chunk(panel):
                c = CHUNKS - 1
                for b in range(BANKS):
                    if b % 2:
                        pe.wait_ge(hi_ready, half_done(panel, 0, c, b // 2))
                    else:
                        pe.wait_ge(part_hi_ready, panel * (BANKS // 2) + (b // 2 + 1))
                    products(b, c, h_lo, hi, c % HI_BUFS)
                    products(b, c, h_hi, hi, c % HI_BUFS)
                    if b % 2:
                        pe.wait_ge(lo_ready, half_done(panel, 0, c, b // 2))
                    else:
                        pe.wait_ge(part_lo_ready, panel * (BANKS // 2) + (b // 2 + 1))
                    products(b, c, h_hi, lo, c % LO_BUFS).then_inc(
                        chunk_used if b == BANKS - 1 else part_sums_ready, 1)

            def biases(panel):
                for b in range(BANKS):
                    pe.wait_ge(y_ready, panel * BANKS + (b + 1))
                    nc.tensor.matmul(outs[:, b], ones[:, :], bias_split[:, :, :], start=True, stop=False)

            def outputs(panel):
                for b in range(BANKS):
                    pe.wait_ge(agg_ready, panel * BANKS + (b + 1))
                    for t in range(BANK_TILES):
                        last = nc.tensor.matmul(outs[:, b, t, :], agg_t[:, b, t * P:(t + 1) * P], w_sb[:, :],
                                                start=False, stop=t == BANK_TILES - 1)
                    last.then_inc(out_ready, 1)

            for c in range(NATIVE):
                native_chunk(c)
            for c in range(NATIVE, CHUNKS - 1):
                if c % NORM_TILES == 0:
                    pe.wait_ge(h_ready, (c - NATIVE) // NORM_TILES + 1)
                if c == BIAS_CHUNK:
                    pe.wait_ge(bias_ready, 2)
                    biases(0)
                chunk(0, c)
            last_chunk(0)
            pe.wait_ge(weight_landed, 16)
            outputs(0)
            pe.wait_ge(h_ready, SPLITS)
            with pe.Fori(1, PANELS) as s:
                for c in range(CHUNKS - 1):
                    if c == BIAS_CHUNK:
                        biases(s)
                    chunk(s, c)
                last_chunk(s)
                outputs(s)


def kernel(x, adj, L0_gnn_kernel, L0_gnn_bias):
    import numpy as np
    import concourse.bacc as bacc
    from concourse import mybir as mb
    from concourse.bass_utils import run_bass_kernel_spmd

    x, adj = np.asarray(x), np.asarray(adj)
    rows = x.shape[0]
    tiles, panels = rows // P, rows // PANEL
    adj_t = adj.reshape(P, panels, PANEL // P, P, tiles).transpose(1, 4, 3, 2, 0)
    arrays = {
        "x_dram": x,
        "adj_dram": np.ascontiguousarray(adj_t).reshape(panels, tiles, P, PANEL),
        "weight_dram": np.asarray(L0_gnn_kernel),
        "bias_dram": np.asarray(L0_gnn_bias),
    }
    arrays = {name: np.ascontiguousarray(a) for name, a in arrays.items()}
    nc = bacc.Bacc("TRN2", target_bir_lowering=False, num_devices=1)
    ins = [nc.dram_tensor(name, a.shape, mb.dt.from_np(a.dtype), kind="ExternalInput").ap() for name, a in arrays.items()]
    out = nc.dram_tensor("out_dram", [rows, arrays["weight_dram"].shape[1]], mb.dt.float32, kind="ExternalOutput").ap()
    gnn_layer(nc, *ins, out)
    r = run_bass_kernel_spmd(nc, [arrays], core_ids=[0])
    return r.results[0]["out_dram"]
```
